# Optimizing a Trainium2 kernel written in Bass

```python
import numpy as np
import jax
import jax.numpy as jnp

def _softmax(x, axis=-1):
    return jax.nn.softmax(x, axis=axis)

def _gelu(x):
    return jax.nn.gelu(x, approximate=True)

def _silu(x):
    return jax.nn.silu(x)

def _sigmoid(x):
    return jax.nn.sigmoid(x)

def _layernorm(x, axis=-1, eps=1e-05):
    m = jnp.mean(x, axis=axis, keepdims=True)
    v = jnp.var(x, axis=axis, keepdims=True)
    return (x - m) / jnp.sqrt(v + eps)

def _scatter_add(tgt, idx, src, axis=0):
    return tgt.at[idx].add(src)

def _segment_sum(src, seg, n):
    return jax.ops.segment_sum(src, seg, n)
kernel_name = 'mk_cond_seq_d1_seqx_r8_b9d908'

def setup_inputs(seed: int=0):
    np.random.seed(seed)
    _w = jnp.asarray

    def _rec_inputs():
        import jax
        import jax.numpy as jnp
        _rk = jax.random.key(seed)
        x = 7.22e-05 + 1 * jax.random.normal(jax.random.fold_in(_rk, 1), (8, 128, 256), jnp.float32)
        _lenS = 128 - jax.random.randint(jax.random.fold_in(_rk, 7), (8,), 0, max(1, 128 // 4) + 1, jnp.int32)
        _lenS2 = 128 - jax.random.randint(jax.random.fold_in(_rk, 8), (8,), 0, max(1, 128 // 4) + 1, jnp.int32)
        cond_2048 = 0.0061147 + 1.02565 * jax.random.normal(jax.random.fold_in(_rk, 11), (8, 256), jnp.float32)
        _validS = jnp.arange(128)[None, :] < _lenS[:, None]
        _validS2 = jnp.arange(128)[None, :] < _lenS2[:, None]
        _causal = jnp.tril(jnp.ones((128, 128), dtype=bool))
        mask_1x1xSxS_ff0 = jnp.where(jnp.ones((1, 1, 128, 128), dtype=bool), 0.0, -1000000000.0).astype(jnp.float32)
        return (x, cond_2048, mask_1x1xSxS_ff0)
    x, cond_2048, mask_1x1xSxS_ff0 = _rec_inputs()

    def _L0_cond_setup():
        import jax, jax.numpy as jnp
        import numpy as np
        B, L, C, H = (2, 256, 256, 16)
        COND = 256
        HID = 4 * C
        LN_EPS = 1e-06

        def _ln(x):
            m = jnp.mean(x, axis=-1, keepdims=True)
            v = jnp.mean((x - m) ** 2, axis=-1, keepdims=True)
            return (x - m) / jnp.sqrt(v + LN_EPS)

        def _gelu_tanh(u):
            c = np.sqrt(2.0 / np.pi).astype(np.float32)
            return 0.5 * u * (1.0 + jnp.tanh(c * (u + 0.044715 * u ** 3)))
        key = jax.random.key(seed)
        ks = jax.random.split(key, 8)
        s = 0.02
        return {'x': jax.random.normal(ks[0], (B, L, C), jnp.float32), 'cond_BD': jax.random.normal(ks[1], (B, COND), jnp.float32), 'attn_bias': jnp.zeros((1, 1, L, L), jnp.float32), 'Wqkv': jax.random.normal(ks[2], (3 * C, C), jnp.float32) * s, 'q_bias': jnp.zeros((C,), jnp.float32), 'v_bias': jnp.zeros((C,), jnp.float32), 'scale_mul_log': jnp.full((1, H, 1, 1), np.log(4.0), jnp.float32), 'Wproj': jax.random.normal(ks[3], (C, C), jnp.float32) * s, 'bproj': jnp.zeros((C,), jnp.float32), 'Wada': jax.random.normal(ks[4], (6 * C, COND), jnp.float32) * s, 'bada': jnp.zeros((6 * C,), jnp.float32), 'Wfc1': jax.random.normal(ks[5], (HID, C), jnp.float32) * s, 'bfc1': jnp.zeros((HID,), jnp.float32), 'Wfc2': jax.random.normal(ks[6], (C, HID), jnp.float32) * s, 'bfc2': jnp.zeros((C,), jnp.float32)}
    _L0_cond_all = _L0_cond_setup()
    _L0_cond_in = {k: v for k, v in _L0_cond_all.items() if k in ('Wqkv', 'q_bias', 'v_bias', 'scale_mul_log', 'Wproj', 'bproj', 'Wada', 'bada', 'Wfc1', 'bfc1', 'Wfc2', 'bfc2')}
    del _L0_cond_all
    return {'x': x, 'cond_2048': cond_2048, 'mask_1x1xSxS_ff0': mask_1x1xSxS_ff0, 'L0_cond_Wqkv': _L0_cond_in['Wqkv'], 'L0_cond_q_bias': _L0_cond_in['q_bias'], 'L0_cond_v_bias': _L0_cond_in['v_bias'], 'L0_cond_scale_mul_log': _L0_cond_in['scale_mul_log'], 'L0_cond_Wproj': _L0_cond_in['Wproj'], 'L0_cond_bproj': _L0_cond_in['bproj'], 'L0_cond_Wada': _L0_cond_in['Wada'], 'L0_cond_bada': _L0_cond_in['bada'], 'L0_cond_Wfc1': _L0_cond_in['Wfc1'], 'L0_cond_bfc1': _L0_cond_in['bfc1'], 'L0_cond_Wfc2': _L0_cond_in['Wfc2'], 'L0_cond_bfc2': _L0_cond_in['bfc2']}

def reference(x, cond_2048, mask_1x1xSxS_ff0, L0_cond_Wqkv, L0_cond_q_bias, L0_cond_v_bias, L0_cond_scale_mul_log, L0_cond_Wproj, L0_cond_bproj, L0_cond_Wada, L0_cond_bada, L0_cond_Wfc1, L0_cond_bfc1, L0_cond_Wfc2, L0_cond_bfc2):
    import jax
    import jax.numpy as jnp

    def _L0_cond_ref(x, cond_BD, attn_bias, Wqkv, q_bias, v_bias, scale_mul_log, Wproj, bproj, Wada, bada, Wfc1, bfc1, Wfc2, bfc2):
        import jax, jax.numpy as jnp
        import numpy as np
        B, L, C, H = (2, 256, 256, 16)
        COND = 256
        HID = 4 * C
        LN_EPS = 1e-06

        def _ln(x):
            m = jnp.mean(x, axis=-1, keepdims=True)
            v = jnp.mean((x - m) ** 2, axis=-1, keepdims=True)
            return (x - m) / jnp.sqrt(v + LN_EPS)

        def _gelu_tanh(u):
            c = np.sqrt(2.0 / np.pi).astype(np.float32)
            return 0.5 * u * (1.0 + jnp.tanh(c * (u + 0.044715 * u ** 3)))
        Bs, Lx, Cx = x.shape
        D = Cx // H
        ada = (jax.nn.silu(cond_BD) @ Wada.T + bada).reshape(Bs, 1, 6, Cx)
        gamma1, gamma2, scale1, scale2, shift1, shift2 = [ada[:, :, i, :] for i in range(6)]

        def attn(xin):
            qkv_bias = jnp.concatenate([q_bias, jnp.zeros_like(q_bias), v_bias])
            qkv = (xin @ Wqkv.T + qkv_bias).reshape(Bs, Lx, 3, H, D)
            qkv = jnp.transpose(qkv, (2, 0, 3, 1, 4))
            q, k, v = (qkv[0], qkv[1], qkv[2])
            sm = jnp.exp(jnp.minimum(scale_mul_log, jnp.log(jnp.float32(100.0))))
            qn = q / jnp.maximum(jnp.linalg.norm(q, axis=-1, keepdims=True), 1e-12) * sm
            kn = k / jnp.maximum(jnp.linalg.norm(k, axis=-1, keepdims=True), 1e-12)
            scores = jnp.einsum('bhqd,bhkd->bhqk', qn, kn) + attn_bias
            p = jax.nn.softmax(scores, axis=-1)
            o = jnp.einsum('bhqk,bhkd->bhqd', p, v)
            o = jnp.transpose(o, (0, 2, 1, 3)).reshape(Bs, Lx, Cx)
            return o @ Wproj.T + bproj
        x = x + attn(_ln(x) * (scale1 + 1.0) + shift1) * gamma1
        h = _gelu_tanh((_ln(x) * (scale2 + 1.0) + shift2) @ Wfc1.T + bfc1)
        x = x + (h @ Wfc2.T + bfc2) * gamma2
        return x
    x = _L0_cond_ref(x, cond_2048, mask_1x1xSxS_ff0, L0_cond_Wqkv, L0_cond_q_bias, L0_cond_v_bias, L0_cond_scale_mul_log, L0_cond_Wproj, L0_cond_bproj, L0_cond_Wada, L0_cond_bada, L0_cond_Wfc1, L0_cond_bfc1, L0_cond_Wfc2, L0_cond_bfc2)
    return x

_drawn_inputs = setup_inputs


def setup_inputs(seed=0):
    import zlib

    import numpy as np

    out = dict(_drawn_inputs(seed))
    spreads = {'L0_cond_q_bias': (0.0, 0.8),
     'L0_cond_v_bias': (0.0, 0.8),
     'L0_cond_scale_mul_log': (1.3862943649291992, 0.6),
     'L0_cond_bproj': (0.0, 0.371),
     'L0_cond_bada': (0.0, 0.415),
     'L0_cond_bfc1': (0.0, 0.8),
     'L0_cond_bfc2': (0.0, 0.374)}
    factors = {'L0_cond_Wqkv': 8.0, 'L0_cond_Wproj': 6.122}
    for name, (base, spread) in spreads.items():
        noise = np.random.default_rng([zlib.crc32(name.encode()), seed]).standard_normal(out[name].shape)
        drawn = base * np.exp(spread * noise) if base else spread * noise
        out[name] = jnp.asarray(drawn.astype(out[name].dtype))
    for name, factor in factors.items():
        out[name] = (out[name] * factor).astype(out[name].dtype)
    return out
```

```python
from contextlib import ExitStack

import numpy as np

import concourse.bass as bass
from concourse import mybir

F32 = mybir.dt.float32
F16 = mybir.dt.float16
BF16 = mybir.dt.bfloat16
I32 = mybir.dt.int32
ALU = mybir.AluOpType
ACT = mybir.ActivationFunctionType
AX = mybir.AxisListType

P = 128
B, S, C, H = 8, 128, 256, 16
D = C // H
HID = 4 * C
KC = C // P
KH = HID // P
NPAIR = B // 2
GT = 4
UH = 4
UB = H // UH
NU = B * UB
NPART = 4
VW = 3 * D + 1
LN_EPS = 1e-6
NORM_EPS = 1e-12
LOG_MAX = float(np.log(np.float32(100.0)))
F32_MAX = 3.4e38
RSQRT_MAGIC = 1597463007.0
NEWTON = 3
GELU_IN = float(np.sqrt(2.0 / np.pi).astype(np.float32))
GELU_CUBE = 0.044715

SMALL = {}
_at = 0
for _name, _n in (("cond", KC * B), ("bada", 12), ("bproj", KC), ("bfc1", KH), ("bfc2", KC), ("log_scale", H),
                  ("mask", S), ("ident", P), ("qk_bias", C), ("v_bias", C)):
    SMALL[_name] = (_at, _at + _n)
    _at += _n
SMALL_N = _at
S1, SH1, G1, S2, SH2, G2 = (KC * i for i in range(6))
ADA_ORDER = (2, 4, 0, 3, 5, 1)


def heads_of(n):
    u = n % UB
    return [8 * (u // 2) + 2 * i + u % 2 for i in range(UH)]


UNIT_STEPS = {
    "scores": -0.22, "max": -0.05, "exp": 0.86, "flip_p": 1.24, "p_hi": 1.26, "p_lo": 1.29, "values": 2.12, "o": 2.07,
}
BATCH_STEPS = {
    "norm1": -9.07, "flip_x": -7.76, "modulate1": -7.0, "qkv": -6.47, "read_qkv": -6.46, "square": -6.63,
    "sums": -6.07, "qk_norm": -4.37, "unit": -4.62, "stack_hi": -3.61, "stack_lo": -3.21, "flip_q": -1.91,
    "read_q": -1.23, "flip_k": -1.09, "read_k": -0.69, "v_parts": -5.43,
}
FIRST_STEPS = {
    "norm1": -3.89, "flip_x": -4.86, "modulate1": -3.81, "qkv": -2.23, "read_qkv": -2.51, "square": -2.62,
    "sums": -2.23, "qk_norm": -2.28, "unit": -1.46, "stack_hi": -1.32, "stack_lo": -1.03, "flip_q": -0.99,
    "read_q": -0.81, "flip_k": -0.27, "read_k": -0.74, "v_parts": -1.79,
}
SECOND_STEPS = {
    "norm1": -2.71, "flip_x": -3.23, "modulate1": -2.87, "qkv": -1.98, "read_qkv": -1.59, "square": -1.89,
    "sums": -1.59, "qk_norm": -1.69, "unit": -0.47, "stack_hi": 0.0, "stack_lo": -0.13, "flip_q": 0.22,
    "read_q": 0.44, "flip_k": 0.39, "read_k": 0.48, "v_parts": -1.56,
}
BATCH_END_STEPS = {
    "flip_o": 2.85, "read_o": 2.94, "proj": 3.3, "x1": 3.94, "flip_x1": 4.68, "read_x1": 5.14, "stats2": 5.32,
    "norm2": 6.69, "flip_h2": 7.31, "modulate2": 7.8,
}
TILE_STEPS = {
    "fc1": (8.01, 0.329), "gelu": (9.76, 1.951), "fc2": (10.66, 0.29),
}
END_STEPS_5 = {
    "flip_o": 2.86, "read_o": 3.04, "proj": 3.3, "x1": 3.39, "flip_x1": 4.9, "read_x1": 5.39, "stats2": 5.88,
    "norm2": 6.83, "flip_h2": 7.5, "modulate2": 7.45,
}
TILE_STEPS_5 = {
    "fc1": (7.86, 0.075), "gelu": (8.6, 0.768), "fc2": (9.63, 0.182),
}
END_STEPS_6 = {
    "flip_o": 2.54, "read_o": 2.68, "proj": 3.04, "x1": 2.99, "flip_x1": 3.7, "read_x1": 3.75, "stats2": 3.79,
    "norm2": 4.13, "flip_h2": 4.39, "modulate2": 4.65,
}
TILE_STEPS_6 = {
    "fc1": (5.19, 0.129), "gelu": (6.11, 0.869), "fc2": (7.4, 0.106),
}
END_STEPS_7 = {
    "flip_o": 2.18, "read_o": 2.23, "proj": 2.33, "x1": 2.56, "flip_x1": 2.67, "read_x1": 2.66, "stats2": 2.65,
    "norm2": 3.43, "flip_h2": 2.99, "modulate2": 3.06,
}
TILE_STEPS_7 = {
    "fc1": (3.67, 0.047), "gelu": (5.12, 0.547), "fc2": (4.87, 0.071),
}
OUT_AFTER = 0.3
STATS_AT = (-10.52, -2.67, -2.55, 4.74)
ADA_AT = (-7.22, -1.11)


def plan():
    steps = [(t, "stats1", p) for p, t in enumerate(STATS_AT)] + [(t, "ada", i) for i, t in enumerate(ADA_AT)]
    for n in range(NU):
        steps += [(n + t, name, n) for name, t in UNIT_STEPS.items() if name != "o" or n % 2]
    starts = {0: FIRST_STEPS, 1: SECOND_STEPS}
    ends = {B - 3: (END_STEPS_5, TILE_STEPS_5), B - 2: (END_STEPS_6, TILE_STEPS_6), B - 1: (END_STEPS_7, TILE_STEPS_7)}
    for b in range(B):
        first = UB * b if b >= 2 else 0
        steps += [(first + t, name, b) for name, t in starts.get(b, BATCH_STEPS).items()]
        end = UB * b + UB - 1
        batch_end, tiles = ends.get(b, (BATCH_END_STEPS, TILE_STEPS))
        steps += [(end + t, name, b) for name, t in batch_end.items()]
        for name, (t, every) in tiles.items():
            steps += [(end + t + every * m, name, (b, m)) for m in range(KH // GT if name == "gelu" else KH)]
        t, every = tiles["fc2"]
        steps.append((end + t + every * (KH - 1) + OUT_AFTER, "out", b))
    return [step[1:] for step in sorted(steps, key=lambda step: step[0])]


SCHEDULE = plan()


def block_kernel(nc: bass.Bass, x_tok, x_T, small, w_ada, w_qkv, w_proj, w_fc1, w_fc2, out):
    with ExitStack() as ctx:
        def sb(name, shape, dt=F32):
            return ctx.enter_context(nc.sbuf_tensor(name, shape, dt))

        def bank(name):
            return ctx.enter_context(nc.psum_tensor(name, [P, 512], F32))

        def sem(name):
            return ctx.enter_context(nc.semaphore(name))

        ps_misc = bank("ps_misc")
        ps_qk = bank("ps_qk")
        ps_u = [bank("ps_u0"), bank("ps_u1")]
        ps_o = bank("ps_o")
        ps_f1 = [bank("ps_f1a"), bank("ps_f1b")]
        ps_f2 = bank("ps_f2")

        sm = sb("sm", [P, SMALL_N])
        wada = sb("wada", [P, 12, KC, P])
        wqkv = sb("wqkv", [P, KC, 3 * C])
        wproj = sb("wproj", [P, KC, C])
        wfc1 = sb("wfc1", [P, KC, HID])
        wfc2 = sb("wfc2", [P, KH, C])

        def par(name):
            a, b = SMALL[name]
            return sm[:, a:b]

        cond = par("cond").rearrange("p (k b) -> p k b", k=KC)
        bada, bproj, bfc1, bfc2 = par("bada"), par("bproj"), par("bfc1"), par("bfc2")
        mask, ident = par("mask"), par("ident")
        ident16 = sb("ident16", [P, P], F16)
        bias_qk = sb("bias_qk", [P, 2 * C])
        silu_e = sb("silu_e", [P, KC, B])
        silu_r = sb("silu_r", [P, KC, B])
        silu = sb("silu", [P, KC, B])
        ada = sb("ada", [P, 12, B])
        g1b = sb("g1b", [P, KC, B])
        g2b = sb("g2b", [P, KC, B])
        scale_h = sb("scale_h", [P, H])
        log_c = sb("log_c", [P, H])

        xn = sb("xn", [P, B, C])
        xT = sb("xT", [P, KC, B * S])
        st6 = sb("st6", [P, 2, B, 6])
        mv = sb("mv", [P, 2, B, 2])
        rstd = sb("rstd", [P, 2, B])
        ln_a = sb("ln_a", [P, 2, B])
        ln_h = sb("ln_h", [P, B])
        ln_t = sb("ln_t", [P, 2, B])
        h1T = sb("h1T", [P, 2, KC, S])
        qk = sb("qk", [P, 4, 2, H, D])
        qk_sq = sb("qk_sq", [P, 2, 2 * H, D])
        ss = sb("ss", [P, B, 2 * H])
        qk_y = sb("qk_y", [P, B, 2 * H])
        qk_t = sb("qk_t", [P, B, 2 * H])
        v_sb = sb("v_sb", [P, 2, H, D])
        v_mid = sb("v_mid", [P, 2, H, D])
        v3 = sb("v3", [P, 4, H, VW], BF16)
        stack = sb("stack", [P, 2, 2, H, NPART, D], F16)
        qT = sb("qT", [P, 4, 8, S], F16)
        kT = sb("kT", [P, 4, 8, S], F16)
        nmax = sb("nmax", [P, 2, UH])
        e = sb("e", [P, 2, UH, S])
        pT_hi = sb("pT_hi", [P, 2, UH, S], F16)
        pT_lo = sb("pT_lo", [P, 2, UH, S], F16)
        o_sum = sb("o_sum", [P, 2, 8, D])
        o_rec = sb("o_rec", [P, 2, 8])
        o = sb("o", [P, 2, H, D])
        oT = sb("oT", [P, 2, KC, S])
        x1T = sb("x1T", [P, KC, B * S])
        x1n = sb("x1n", [P, 2, C])
        h2T = sb("h2T", [P, 2, KC, S])
        u = sb("u", [P, 4, GT, S])
        u_sq = sb("u_sq", [P, 2, GT, S])
        u_in = sb("u_in", [P, 2, GT, S])
        u_th = sb("u_th", [P, 2, GT, S])
        hidT = sb("hidT", [P, 2, KH, S])
        g2h = sb("g2h", [P, KC, B])
        outT = sb("outT", [P, 2, KC, S])

        small_in = sem("small_in")
        ada_in = [sem("ada_in0"), sem("ada_in1")]
        x_in = [sem(f"x_in{p}") for p in range(NPAIR)]
        xT_in = sem("xT_in")
        wqkv_in, wproj_in, wfc1_in, wfc2_in = sem("wqkv_in"), sem("wproj_in"), sem("wfc1_in"), sem("wfc2_in")
        out_done = [sem("out_done0"), sem("out_done1")]
        consts = sem("consts")
        ones_set = sem("ones_set")
        silu_exp = sem("silu_exp")
        silu_done = sem("silu_done")
        scale_done = sem("scale_done")
        ada_ps = sem("ada_ps")
        ada_done = sem("ada_done")
        stats1 = sem("stats1")
        xn_done = sem("xn_done")
        xnT_ps = sem("xnT_ps")
        h1_done = sem("h1_done")
        qk_ps = sem("qk_ps")
        v_ps = sem("v_ps")
        qk_sb = sem("qk_sb")
        v_done = sem("v_done")
        sq_done = sem("sq_done")
        ss_done = sem("ss_done")
        qk_rs = sem("qk_rs")
        v_hi = sem("v_hi")
        v_split = sem("v_split")
        qkn = sem("qkn")
        stack_hi = sem("stack_hi")
        stack_lo = sem("stack_lo")
        qT_ps = sem("qT_ps")
        kT_ps = sem("kT_ps")
        qT_done = sem("qT_done")
        kT_done = sem("kT_done")
        s_ps = sem("s_ps")
        s_max = sem("s_max")
        e_done = sem("e_done")
        pT_ps = sem("pT_ps")
        p_hi = sem("p_hi")
        p_lo = sem("p_lo")
        o_ps = sem("o_ps")
        o_done = sem("o_done")
        oT_ps = sem("oT_ps")
        oT_done = sem("oT_done")
        xg1 = sem("xg1")
        xg2 = sem("xg2")
        proj_ps = sem("proj_ps")
        x1_done = sem("x1_done")
        x1t_ps = sem("x1t_ps")
        x1t_done = sem("x1t_done")
        stats2 = sem("stats2")
        rstd2 = sem("rstd2")
        x1n_done = sem("x1n_done")
        x1nT_ps = sem("x1nT_ps")
        h2_done = sem("h2_done")
        fc1_ps = sem("fc1_ps")
        u_done = sem("u_done")
        sq2_done = sem("sq2_done")
        in_done = sem("in_done")
        tanh_done = sem("tanh_done")
        hid_done = sem("hid_done")
        fc2_ps = sem("fc2_ps")
        y_done = sem("y_done")
        dve_step = sem("dve_step")
        pool_step = sem("pool_step")

        def cols(b):
            return slice(b * S, (b + 1) * S)

        block = ctx.enter_context(nc.Block())

        @block.sync
        def _(sp):
            sp.dma_start(sm[:], small).then_inc(small_in, 16)
            sp.dma_start(xn[:, 0:2, :], x_tok[:, 0:2, :]).then_inc(x_in[0], 16)
            sp.dma_start(wada[:, 0:4], w_ada[:, 0:4]).then_inc(ada_in[0], 16)
            sp.dma_start(wqkv[:], w_qkv).then_inc(wqkv_in, 16)
            for p in range(1, NPAIR):
                sp.dma_start(xn[:, 2 * p:2 * p + 2, :], x_tok[:, 2 * p:2 * p + 2, :]).then_inc(x_in[p], 16)
            sp.dma_start(wada[:, 4:12], w_ada[:, 4:12]).then_inc(ada_in[1], 16)
            sp.dma_start(xT[:], x_T).then_inc(xT_in, 16)
            sp.dma_start(wproj[:], w_proj).then_inc(wproj_in, 16)
            sp.dma_start(wfc1[:], w_fc1).then_inc(wfc1_in, 16)
            sp.dma_start(wfc2[:], w_fc2).then_inc(wfc2_in, 16)
            for b in range(B):
                sp.wait_ge(y_done, b + 1)
                sp.dma_start(out[:, :, cols(b)], outT[:, b % 2]).then_inc(out_done[b % 2], 16)
            for r in range(2):
                sp.wait_ge(out_done[r], 16 * (B // 2))

        @block.gpsimd
        def _(pool):
            count = [0]

            def link(ins):
                count[0] += 1
                ins.then_inc(pool_step, 1)
                pool.wait_ge(pool_step, count[0])

            def rsqrt_steps(x, y, t):
                for it in range(NEWTON):
                    link(nc.gpsimd.tensor_tensor(t, y, y, ALU.mult))
                    link(nc.gpsimd.tensor_tensor(t, t, x, ALU.mult))
                    link(nc.gpsimd.tensor_scalar(t, t, -0.5, 1.5, ALU.mult, ALU.add))
                    last = nc.gpsimd.tensor_tensor(y, y, t, ALU.mult)
                    if it < NEWTON - 1:
                        link(last)
                return last

            def rsqrt_column(x_half, y, t):
                for it in range(NEWTON):
                    link(nc.gpsimd.tensor_scalar(t, y, y, x_half, ALU.mult, ALU.mult))
                    last = nc.gpsimd.tensor_scalar(y, t, 1.5, y, ALU.add, ALU.mult)
                    if it < NEWTON - 1:
                        link(last)
                return last

            nc.gpsimd.memset(v3[:, :, :, 3 * D:VW], 1.0).then_inc(ones_set, 1)

            for step, i in SCHEDULE:
                if step == "stats1":
                    pool.wait_ge(stats1, i + 1)
                    b = slice(2 * i, 2 * i + 2)
                    link(rsqrt_steps(ln_a[:, 0, b], rstd[:, 0, b], ln_t[:, 0, b]))
                elif step == "norm1":
                    nc.gpsimd.tensor_scalar(xn[:, i], xn[:, i], mv[:, 0, i, 0:1], rstd[:, 0, i:i + 1],
                                            ALU.subtract, ALU.mult).then_inc(xn_done, 1)
                elif step == "v_parts":
                    pool.wait_ge(v_hi, i + 1)
                    r, w = i % 2, i % 4
                    link(nc.gpsimd.tensor_tensor(v_mid[:, r], v_sb[:, r], v3[:, w, :, 0:D], ALU.subtract))
                    link(nc.gpsimd.tensor_scalar(v3[:, w, :, D:2 * D], v_mid[:, r], 1.0, None, ALU.mult))
                    nc.gpsimd.tensor_tensor(v3[:, w, :, 2 * D:3 * D], v_mid[:, r], v3[:, w, :, D:2 * D],
                                            ALU.subtract).then_inc(v_split, 1)
                elif step == "qk_norm":
                    pool.wait_ge(ss_done, i + 1)
                    if i == 0:
                        pool.wait_ge(scale_done, 1)
                    link(rsqrt_steps(ss[:, i], qk_y[:, i], qk_t[:, i]))
                    nc.gpsimd.tensor_tensor(qk_y[:, i, 0:H], qk_y[:, i, 0:H], scale_h[:], ALU.mult).then_inc(qk_rs, 1)
                elif step == "proj":
                    if i == 0:
                        pool.wait_ge(xT_in, 16)
                        pool.wait_ge(ada_done, 3)
                    for m in range(KC):
                        last = nc.gpsimd.tensor_scalar(xT[:, m, cols(i)], xT[:, m, cols(i)], g1b[:, m, i:i + 1],
                                                       None, ALU.add)
                    last.then_inc(xg1, 1)
                elif step == "read_x1":
                    pool.wait_ge(x1_done, i + 1)
                    for m in range(KC):
                        last = nc.gpsimd.tensor_scalar(xT[:, m, cols(i)], x1T[:, m, cols(i)], g2b[:, m, i:i + 1],
                                                       None, ALU.add)
                    last.then_inc(xg2, 1)
                elif step == "stats2":
                    pool.wait_ge(stats2, i + 1)
                    b = slice(i, i + 1)
                    rsqrt_column(ln_h[:, b], rstd[:, 1, b], ln_t[:, 1, b]).then_inc(rstd2, 1)
                elif step == "fc1" and i[1] % GT == GT - 1:
                    n = (KH * i[0] + i[1]) // GT
                    pool.wait_ge(u_done, GT * n + GT)
                    if n >= 2:
                        pool.wait_ge(in_done, n - 1)
                    nc.gpsimd.tensor_tensor(u_sq[:, n % 2], u[:, n % 4], u[:, n % 4], ALU.mult).then_inc(sq2_done, 1)

        @block.scalar
        def _(act):
            act.wait_ge(small_in, 16)
            nc.scalar.activation(silu_e[:], cond, ACT.Exp, scale=-1.0).then_inc(silu_exp, 1)
            act.wait_ge(consts, 1)
            nc.scalar.activation(scale_h[:], log_c[:], ACT.Exp).then_inc(scale_done, 1)
            for step, i in SCHEDULE:
                if step == "modulate1":
                    act.wait_ge(xnT_ps, i + 1)
                    if i == 0:
                        act.wait_ge(ada_done, 1)
                    if i >= 2:
                        act.wait_ge(v_ps, i - 1)
                    for k in range(KC):
                        last = nc.scalar.activation(h1T[:, i % 2, k], ps_misc[:, k * S:(k + 1) * S], ACT.Identity,
                                                    bias=ada[:, SH1 + k, i:i + 1], scale=ada[:, S1 + k, i:i + 1])
                    last.then_inc(h1_done, 1)
                elif step == "square":
                    act.wait_ge(qk_sb, i + 1)
                    if i >= 2:
                        act.wait_ge(ss_done, i - 1)
                    nc.scalar.activation(qk_sq[:, i % 2], qk[:, i % 4].rearrange("p a h d -> p (a h) d"),
                                         ACT.Square).then_inc(sq_done, 1)
                    act.wait_ge(v_done, i + 1)
                    if i >= 4:
                        act.wait_ge(o_ps, UB * (i - 3))
                    nc.scalar.copy(v3[:, i % 4, :, 0:D], v_sb[:, i % 2]).then_inc(v_hi, 1)
                elif step == "stack_hi":
                    act.wait_ge(qkn, i + 1)
                    if i >= 2:
                        act.wait_ge(kT_ps, i - 1)
                    nc.scalar.copy(stack[:, i % 2, 0, :, 0:2],
                                   qk[:, i % 4, 0].unsqueeze(2).broadcast_to([P, H, 2, D])).then_inc(stack_hi, 1)
                    nc.scalar.copy(stack[:, i % 2, 1, :, 0:4:2],
                                   qk[:, i % 4, 1].unsqueeze(2).broadcast_to([P, H, 2, D])).then_inc(stack_hi, 1)
                elif step == "read_q":
                    act.wait_ge(qT_ps, i + 1)
                    if i >= 4:
                        act.wait_ge(s_ps, UB * (i - 3))
                    nc.scalar.copy(qT[:, i % 4], ps_qk[:, :].bitcast(F16).rearrange("p (j s) -> p j s", s=S)
                                   ).then_inc(qT_done, 1)
                elif step == "exp":
                    act.wait_ge(s_max, i + 1)
                    if i >= 2:
                        act.wait_ge(pT_ps, i - 1)
                    for h in range(UH):
                        last = nc.scalar.activation(e[:, i % 2, h], ps_u[i % 2][:, h * S:(h + 1) * S], ACT.Exp,
                                                    scale=-1.0, bias=nmax[:, i % 2, h:h + 1])
                    last.then_inc(e_done, 1)
                elif step == "read_k":
                    act.wait_ge(kT_ps, i + 1)
                    if i >= 4:
                        act.wait_ge(s_ps, UB * (i - 3))
                    nc.scalar.copy(kT[:, i % 4], ps_qk[:, :].bitcast(F16).rearrange("p (j s) -> p j s", s=S)
                                   ).then_inc(kT_done, 1)
                elif step == "p_hi":
                    act.wait_ge(pT_ps, i + 1)
                    if i >= 2:
                        act.wait_ge(o_ps, i - 1)
                    nc.scalar.copy(pT_hi[:, i % 2], ps_u[i % 2][:, :].rearrange("p (h s) -> p h s", h=UH)).then_inc(p_hi, 1)
                elif step == "read_o":
                    act.wait_ge(oT_ps, i + 1)
                    if i >= 2:
                        act.wait_ge(proj_ps, i - 1)
                    nc.scalar.copy(oT[:, i % 2], ps_misc[:, 0:C].rearrange("p (k s) -> p k s", k=KC)).then_inc(oT_done, 1)
                elif step == "read_x1":
                    act.wait_ge(x1t_ps, i + 1)
                    if i >= 2:
                        act.wait_ge(x1nT_ps, i - 1)
                    nc.scalar.copy(x1n[:, i % 2], ps_misc[:, 0:C]).then_inc(x1t_done, 1)
                elif step == "modulate2":
                    act.wait_ge(x1nT_ps, i + 1)
                    if i == 0:
                        act.wait_ge(ada_done, 3)
                    if i >= 2:
                        act.wait_ge(fc1_ps, KH * (i - 1))
                    for k in range(KC):
                        last = nc.scalar.activation(h2T[:, i % 2, k], ps_misc[:, k * S:(k + 1) * S], ACT.Identity,
                                                    bias=ada[:, SH2 + k, i:i + 1], scale=ada[:, S2 + k, i:i + 1])
                    last.then_inc(h2_done, 1)
                elif step == "fc1":
                    b, m = i
                    n = (KH * b + m) // GT
                    act.wait_ge(fc1_ps, KH * b + m + 1)
                    if n >= 4:
                        act.wait_ge(hid_done, n - 3)
                    nc.scalar.activation(u[:, n % 4, m % GT], ps_f1[m % 2][:, 0:S], ACT.Identity,
                                         bias=bfc1[:, m:m + 1]).then_inc(u_done, 1)
                elif step == "gelu":
                    n = KH // GT * i[0] + i[1]
                    act.wait_ge(in_done, n + 1)
                    if n >= 2:
                        act.wait_ge(hid_done, n - 1)
                    nc.scalar.activation(u_th[:, n % 2], u_in[:, n % 2], ACT.Tanh,
                                         scale=GELU_IN * GELU_CUBE).then_inc(tanh_done, 1)

        @block.vector
        def _(dve):
            count = [0]

            def link(ins):
                count[0] += 1
                ins.then_inc(dve_step, 1)
                dve.wait_ge(dve_step, count[0])

            def rsqrt_guess(y, x):
                return nc.vector.tensor_scalar(y.bitcast(I32), x.bitcast(I32), -0.5, RSQRT_MAGIC, ALU.mult, ALU.add)

            def store_gated(b, dst, src, gate, plus):
                for m in range(KC):
                    last = nc.vector.scalar_tensor_tensor(
                        out=dst[:, m], in0=src[:, m * S:(m + 1) * S], scalar=gate[:, m, b:b + 1],
                        in1=plus[:, m, cols(b)], op0=ALU.mult, op1=ALU.add)
                return last

            dve.wait_ge(small_in, 16)
            nc.vector.tensor_scalar(log_c[:], par("log_scale"), LOG_MAX, None, ALU.min).then_inc(consts, 1)
            nc.vector.tensor_copy(bias_qk[:, 0:C], par("qk_bias"))
            nc.vector.memset(bias_qk[:, C:2 * C], 0.0)
            nc.vector.tensor_copy(ident16[:], ident).then_inc(consts, 1)
            dve.wait_ge(silu_exp, 1)
            link(nc.vector.tensor_scalar(silu_r[:], silu_e[:], 1.0, None, ALU.add))
            link(nc.vector.reciprocal(silu_r[:], silu_r[:]))
            nc.vector.tensor_tensor(silu[:], silu_r[:], cond, ALU.mult).then_inc(silu_done, 1)

            for step, i in SCHEDULE:
                if step == "stats1":
                    dve.wait_ge(x_in[i], 16)
                    for b in (2 * i, 2 * i + 1):
                        last = nc.vector.bn_stats(st6[:, 0, b], xn[:, b])
                    link(last)
                    for b in (2 * i, 2 * i + 1):
                        last = nc.vector.bn_aggr(mv[:, 0, b], st6[:, 0, b])
                    link(last)
                    b = slice(2 * i, 2 * i + 2)
                    link(nc.vector.tensor_scalar(ln_a[:, 0, b], mv[:, 0, b, 1], LN_EPS, None, ALU.add))
                    rsqrt_guess(rstd[:, 0, b], ln_a[:, 0, b]).then_inc(stats1, 1)
                elif step == "ada":
                    t = slice(0, 4) if i == 0 else slice(4, 12)
                    n = t.stop - t.start
                    dve.wait_ge(ada_ps, i + 1)
                    link(nc.vector.tensor_tensor(ada[:, t], (ps_f2 if i == 0 else ps_f1[0])[:, 0:n * B].rearrange(
                        "p (t b) -> p t b", b=B), bada[:, t].unsqueeze(2).broadcast_to([P, n, B]), ALU.add))
                    scale = S1 if i == 0 else S2
                    nc.vector.tensor_scalar(ada[:, scale:scale + KC], ada[:, scale:scale + KC], 1.0, None,
                                            ALU.add).then_inc(ada_done, 1)
                    if i == 1:
                        nc.vector.tensor_scalar(g2h[:], ada[:, G2:G2 + KC], 0.5, None, ALU.mult)
                        nc.vector.tensor_tensor(g1b[:], ada[:, G1:G1 + KC], bproj.unsqueeze(2).broadcast_to([P, KC, B]),
                                                ALU.mult)
                        nc.vector.tensor_tensor(g2b[:], ada[:, G2:G2 + KC], bfc2.unsqueeze(2).broadcast_to([P, KC, B]),
                                                ALU.mult).then_inc(ada_done, 1)
                elif step == "read_qkv":
                    dve.wait_ge(qk_ps, i + 1)
                    nc.vector.tensor_tensor(qk[:, i % 4].rearrange("p a h d -> p (a h d)"), ps_qk[:, :], bias_qk[:],
                                            ALU.add).then_inc(qk_sb, 1)
                    dve.wait_ge(v_ps, i + 1)
                    if i >= 2:
                        dve.wait_ge(v_split, i - 1)
                    nc.vector.tensor_tensor(v_sb[:, i % 2].rearrange("p h d -> p (h d)"), ps_misc[:, C:2 * C],
                                            par("v_bias"), ALU.add).then_inc(v_done, 1)
                elif step == "sums":
                    dve.wait_ge(sq_done, i + 1)
                    link(nc.vector.tensor_reduce(ss[:, i], qk_sq[:, i % 2], axis=AX.X, op=ALU.add))
                    link(nc.vector.tensor_scalar(ss[:, i], ss[:, i], NORM_EPS * NORM_EPS, None, ALU.max))
                    rsqrt_guess(qk_y[:, i], ss[:, i]).then_inc(ss_done, 1)
                elif step == "unit":
                    dve.wait_ge(qk_rs, i + 1)
                    nc.vector.tensor_tensor(
                        qk[:, i % 4].rearrange("p a h d -> p (a h) d"), qk[:, i % 4].rearrange("p a h d -> p (a h) d"),
                        qk_y[:, i].unsqueeze(2).broadcast_to([P, 2 * H, D]), ALU.mult).then_inc(qkn, 1)
                elif step == "stack_lo":
                    dve.wait_ge(qkn, i + 1)
                    dve.wait_ge(stack_hi, 2 * i + 1)
                    nc.vector.tensor_tensor(stack[:, i % 2, 0, :, 2:4],
                                            qk[:, i % 4, 0].unsqueeze(2).broadcast_to([P, H, 2, D]),
                                            stack[:, i % 2, 0, :, 0:2], ALU.subtract).then_inc(stack_lo, 1)
                    dve.wait_ge(stack_hi, 2 * i + 2)
                    nc.vector.tensor_tensor(stack[:, i % 2, 1, :, 1:4:2],
                                            qk[:, i % 4, 1].unsqueeze(2).broadcast_to([P, H, 2, D]),
                                            stack[:, i % 2, 1, :, 0:4:2], ALU.subtract).then_inc(stack_lo, 1)
                elif step == "max":
                    dve.wait_ge(s_ps, i + 1)
                    for h in range(UH):
                        sc = ps_u[i % 2][:, h * S:(h + 1) * S]
                        last = nc.vector.tensor_tensor_reduce(
                            out=sc, in0=sc, in1=mask, scale=-1.0, scalar=F32_MAX, op0=ALU.add, op1=ALU.min,
                            accum_out=nmax[:, i % 2, h:h + 1])
                    last.then_inc(s_max, 1)
                elif step == "p_lo":
                    dve.wait_ge(p_hi, i + 1)
                    nc.vector.tensor_tensor(pT_lo[:, i % 2], ps_u[i % 2][:, :].rearrange("p (h s) -> p h s", h=UH),
                                            pT_hi[:, i % 2], ALU.subtract).then_inc(p_lo, 1)
                elif step == "o":
                    half, b = (i % UB) // 2, i // UB
                    dve.wait_ge(o_ps, i + 1)
                    parts = ps_o[:, 0:8 * VW].rearrange("p (h w) -> p h w", w=VW)
                    nc.vector.tensor_reduce(
                        o_sum[:, half], parts[:, :, 0:3 * D].rearrange("p h (t d) -> p h d t", t=3),
                        axis=AX.X, op=ALU.add)
                    link(nc.vector.reciprocal(o_rec[:, half], parts[:, :, 3 * D]))
                    if b >= 2:
                        dve.wait_ge(oT_ps, b - 1)
                    nc.vector.tensor_tensor(o[:, b % 2, 8 * half:8 * half + 8], o_sum[:, half],
                                            o_rec[:, half].unsqueeze(2).broadcast_to([P, 8, D]),
                                            ALU.mult).then_inc(o_done, 1)
                elif step == "x1":
                    dve.wait_ge(proj_ps, i + 1)
                    dve.wait_ge(xg1, i + 1)
                    store_gated(i, x1T[:, :, cols(i)], ps_f1[0], ada[:, G1:G1 + KC], xT).then_inc(x1_done, 1)
                elif step == "stats2":
                    dve.wait_ge(x1t_done, i + 1)
                    link(nc.vector.bn_stats(st6[:, 1, i], x1n[:, i % 2]))
                    link(nc.vector.bn_aggr(mv[:, 1, i], st6[:, 1, i]))
                    nc.vector.tensor_scalar(ln_h[:, i:i + 1], mv[:, 1, i, 1:2], LN_EPS, -0.5, ALU.add, ALU.mult)
                    link(nc.vector.tensor_scalar(ln_a[:, 1, i:i + 1], mv[:, 1, i, 1:2], LN_EPS, None, ALU.add))
                    rsqrt_guess(rstd[:, 1, i:i + 1], ln_a[:, 1, i:i + 1]).then_inc(stats2, 1)
                elif step == "norm2":
                    dve.wait_ge(rstd2, i + 1)
                    nc.vector.tensor_scalar(x1n[:, i % 2], x1n[:, i % 2], mv[:, 1, i, 0:1], rstd[:, 1, i:i + 1],
                                            ALU.subtract, ALU.mult).then_inc(x1n_done, 1)
                elif step == "fc1" and i[1] % GT == GT - 1:
                    n = (KH * i[0] + i[1]) // GT
                    dve.wait_ge(sq2_done, n + 1)
                    if n >= 2:
                        dve.wait_ge(tanh_done, n - 1)
                    nc.vector.scalar_tensor_tensor(out=u_in[:, n % 2], in0=u_sq[:, n % 2], scalar=1.0 / GELU_CUBE,
                                                   in1=u[:, n % 4], op0=ALU.add, op1=ALU.mult).then_inc(in_done, 1)
                elif step == "gelu":
                    b, g = i
                    n = KH // GT * b + g
                    dve.wait_ge(tanh_done, n + 1)
                    if b >= 2 and g == 0:
                        dve.wait_ge(fc2_ps, b - 1)
                    nc.vector.scalar_tensor_tensor(out=hidT[:, b % 2, GT * g:GT * (g + 1)], in0=u_th[:, n % 2], scalar=1.0,
                                                   in1=u[:, n % 4], op0=ALU.add, op1=ALU.mult).then_inc(hid_done, 1)
                elif step == "out":
                    dve.wait_ge(fc2_ps, i + 1)
                    dve.wait_ge(xg2, i + 1)
                    if i >= 2:
                        dve.wait_ge(out_done[i % 2], 16 * (i // 2))
                    store_gated(i, outT[:, i % 2], ps_f2, g2h, xT).then_inc(y_done, 1)

        @block.tensor
        def _(pe):
            free = {"misc": None, "qk": None, "f1a": None, "f1b": None, "f2": None}

            def take(name, reader, value):
                if free[name] is not None:
                    pe.wait_ge(*free[name])
                free[name] = (reader, value)

            def transpose(dst, src, idn):
                return nc.tensor.matmul(dst, src, idn, is_transpose=True)

            pe.wait_ge(consts, 2)
            for step, i in SCHEDULE:
                if step == "ada":
                    t0, t1 = (0, 4) if i == 0 else (4, 12)
                    if i == 0:
                        pe.wait_ge(silu_done, 1)
                    pe.wait_ge(ada_in[i], 16)
                    take("f2" if i == 0 else "f1a", ada_done, i + 1)
                    dst = ps_f2 if i == 0 else ps_f1[0]
                    for t in range(t0, t1):
                        for k in range(KC):
                            last = nc.tensor.matmul(dst[:, (t - t0) * B:(t - t0 + 1) * B], wada[:, t, k], silu[:, k],
                                                    start=(k == 0), stop=(k == KC - 1))
                    last.then_inc(ada_ps, 1)
                elif step == "flip_x":
                    pe.wait_ge(xn_done, i + 1)
                    take("misc", h1_done, i + 1)
                    for k in range(KC):
                        last = transpose(ps_misc[:, k * S:(k + 1) * S], xn[:, i, k * P:(k + 1) * P], ident)
                    last.then_inc(xnT_ps, 1)
                elif step == "qkv":
                    pe.wait_ge(h1_done, i + 1)
                    if i == 0:
                        pe.wait_ge(wqkv_in, 16)
                    take("qk", qk_sb, i + 1)
                    for k in range(KC):
                        last = nc.tensor.matmul(ps_qk[:, :], h1T[:, i % 2, k], wqkv[:, k, 0:2 * C],
                                                start=(k == 0), stop=(k == KC - 1))
                    last.then_inc(qk_ps, 1)
                    take("misc", v_done, i + 1)
                    for k in range(KC):
                        last = nc.tensor.matmul(ps_misc[:, C:2 * C], h1T[:, i % 2, k], wqkv[:, k, 2 * C:3 * C],
                                                start=(k == 0), stop=(k == KC - 1))
                    last.then_inc(v_ps, 1)
                elif step in ("flip_q", "flip_k"):
                    a, done, reader = (0, qT_ps, qT_done) if step == "flip_q" else (1, kT_ps, kT_done)
                    pe.wait_ge(stack_lo, 2 * i + a + 1)
                    take("qk", reader, i + 1)
                    for j in range(H // 2):
                        last = transpose(ps_qk[:, :].bitcast(F16)[:, j * S:(j + 1) * S],
                                         stack[:, i % 2, a, 2 * j:2 * j + 2].rearrange("p h t d -> p (h t d)"),
                                         ident16[:])
                    last.then_inc(done, 1)
                elif step == "scores":
                    b = i // UB
                    pe.wait_ge(qT_done, b + 1)
                    pe.wait_ge(kT_done, b + 1)
                    if i >= 2:
                        pe.wait_ge(p_lo, i - 1)
                    for n, h in enumerate(heads_of(i)):
                        rows = slice(64 * (h % 2), 64 * (h % 2) + 64)
                        last = nc.tensor.matmul(ps_u[i % 2][:, n * S:(n + 1) * S], qT[rows, b % 4, h // 2],
                                                kT[rows, b % 4, h // 2], start=True, stop=True)
                    last.then_inc(s_ps, 1)
                elif step == "flip_p":
                    pe.wait_ge(e_done, i + 1)
                    for n in range(UH):
                        last = transpose(ps_u[i % 2][:, n * S:(n + 1) * S], e[:, i % 2, n], ident)
                    last.then_inc(pT_ps, 1)
                elif step == "values":
                    b = i // UB
                    pe.wait_ge(p_lo, i + 1)
                    if i == 0:
                        pe.wait_ge(ones_set, 1)
                    pe.wait_ge(v_split, b + 1)
                    if i % 2 == 0 and i >= 2:
                        pe.wait_ge(o_done, i // 2)
                    for n, h in enumerate(heads_of(i)):
                        dst = ps_o[:, (h % 8) * VW:(h % 8 + 1) * VW]
                        nc.tensor.matmul(dst, pT_hi[:, i % 2, n], v3[:, b % 4, h], start=True, stop=False)
                        last = nc.tensor.matmul(dst, pT_lo[:, i % 2, n], v3[:, b % 4, h], start=False, stop=True)
                    last.then_inc(o_ps, 1)
                elif step == "flip_o":
                    pe.wait_ge(o_done, 2 * i + 2)
                    take("misc", oT_done, i + 1)
                    for k in range(KC):
                        last = transpose(ps_misc[:, k * S:(k + 1) * S],
                                         o[:, i % 2, 8 * k:8 * k + 8].rearrange("p h d -> p (h d)"), ident)
                    last.then_inc(oT_ps, 1)
                elif step == "proj":
                    pe.wait_ge(oT_done, i + 1)
                    if i == 0:
                        pe.wait_ge(wproj_in, 16)
                    take("f1a", x1_done, i + 1)
                    for m in range(KC):
                        for k in range(KC):
                            last = nc.tensor.matmul(ps_f1[0][:, m * S:(m + 1) * S], wproj[:, k, m * P:(m + 1) * P],
                                                    oT[:, i % 2, k], start=(k == 0), stop=(k == KC - 1))
                    last.then_inc(proj_ps, 1)
                elif step == "flip_x1":
                    pe.wait_ge(x1_done, i + 1)
                    take("misc", x1t_done, i + 1)
                    for k in range(KC):
                        last = transpose(ps_misc[:, k * P:(k + 1) * P], x1T[:, k, cols(i)], ident)
                    last.then_inc(x1t_ps, 1)
                elif step == "flip_h2":
                    pe.wait_ge(x1n_done, i + 1)
                    take("misc", h2_done, i + 1)
                    for k in range(KC):
                        last = transpose(ps_misc[:, k * S:(k + 1) * S], x1n[:, i % 2, k * P:(k + 1) * P], ident)
                    last.then_inc(x1nT_ps, 1)
                elif step == "fc1":
                    b, m = i
                    pe.wait_ge(h2_done, b + 1)
                    if b == 0 and m == 0:
                        pe.wait_ge(wfc1_in, 16)
                    take("f1b" if m % 2 else "f1a", u_done, KH * b + m + 1)
                    for k in range(KC):
                        last = nc.tensor.matmul(ps_f1[m % 2][:, 0:S], wfc1[:, k, m * P:(m + 1) * P], h2T[:, b % 2, k],
                                                start=(k == 0), stop=(k == KC - 1))
                    last.then_inc(fc1_ps, 1)
                elif step == "fc2":
                    b, m = i
                    pe.wait_ge(hid_done, (KH * b + m) // GT + 1)
                    if m == 0:
                        if b == 0:
                            pe.wait_ge(wfc2_in, 16)
                        take("f2", y_done, b + 1)
                    for c in range(KC):
                        last = nc.tensor.matmul(ps_f2[:, c * S:(c + 1) * S], wfc2[:, m, c * P:(c + 1) * P],
                                                hidT[:, b % 2, m], start=(m == 0 and c == 0), stop=(m == KH - 1),
                                                skip_group_check=True)
                    if m == KH - 1:
                        last.then_inc(fc2_ps, 1)


def kernel(x, cond_2048, mask_1x1xSxS_ff0, L0_cond_Wqkv, L0_cond_q_bias, L0_cond_v_bias, L0_cond_scale_mul_log,
           L0_cond_Wproj, L0_cond_bproj, L0_cond_Wada, L0_cond_bada, L0_cond_Wfc1, L0_cond_bfc1, L0_cond_Wfc2,
           L0_cond_bfc2):
    import concourse.bacc as bacc
    from concourse.bass_utils import run_bass_kernel_spmd

    a = np.asarray

    def weight(w):
        n_out, n_in = w.shape
        return np.ascontiguousarray(a(w).T.reshape(n_in // P, P, n_out).transpose(1, 0, 2))

    def column(v):
        return a(v).reshape(-1, P).T

    def row(v):
        return np.broadcast_to(a(v).reshape(1, -1), (P, a(v).size))

    tiles = [KC * i + k for i in ADA_ORDER for k in range(KC)]
    small = np.concatenate([
        a(cond_2048).T.reshape(KC, P, B).transpose(1, 0, 2).reshape(P, KC * B),
        column(L0_cond_bada)[:, tiles], column(L0_cond_bproj), column(L0_cond_bfc1), column(L0_cond_bfc2),
        row(L0_cond_scale_mul_log), a(mask_1x1xSxS_ff0).reshape(S, S), np.eye(P, dtype=np.float32),
        row(L0_cond_q_bias), row(L0_cond_v_bias)], axis=1)
    w_ada = weight(L0_cond_Wada).reshape(P, KC, 12, P).transpose(0, 2, 1, 3)[:, tiles]
    arrays = {
        "x_tok": a(x).transpose(1, 0, 2),
        "x_T": a(x).reshape(B * S, KC, P).transpose(2, 1, 0),
        "small": small,
        "w_ada": w_ada,
        "w_qkv": weight(L0_cond_Wqkv),
        "w_proj": weight(L0_cond_Wproj),
        "w_fc1": weight(L0_cond_Wfc1),
        "w_fc2": weight(L0_cond_Wfc2),
    }
    arrays = {k: np.ascontiguousarray(v) for k, v in arrays.items()}
    nc = bacc.Bacc("TRN2", target_bir_lowering=False, num_devices=1)
    args = [nc.dram_tensor(k + "_dram", v.shape, F32, kind="ExternalInput").ap() for k, v in arrays.items()]
    out = nc.dram_tensor("out_dram", (P, KC, B * S), F32, kind="ExternalOutput").ap()
    block_kernel(nc, *args, out)
    r = run_bass_kernel_spmd(nc, [{k + "_dram": v for k, v in arrays.items()}], core_ids=[0])
    got = r.results[0]["out_dram"]
    return np.ascontiguousarray(got.transpose(2, 1, 0)).reshape(B, S, C)
```
